# Optimizing a Trainium2 kernel written in Bass

```python
import numpy as np
import jax
import jax.numpy as jnp

def _softmax(x, axis=-1):
    return jax.nn.softmax(x, axis=axis)

def _gelu(x):
    return jax.nn.gelu(x, approximate=True)

def _silu(x):
    return jax.nn.silu(x)

def _sigmoid(x):
    return jax.nn.sigmoid(x)

def _layernorm(x, axis=-1, eps=1e-05):
    m = jnp.mean(x, axis=axis, keepdims=True)
    v = jnp.var(x, axis=axis, keepdims=True)
    return (x - m) / jnp.sqrt(v + eps)

def _scatter_add(tgt, idx, src, axis=0):
    return tgt.at[idx].add(src)

def _segment_sum(src, seg, n):
    return jax.ops.segment_sum(src, seg, n)
kernel_name = 'mk_adj_resnorm_d1_adj_r2_8ff179'

def setup_inputs(seed: int=0):
    np.random.seed(seed)
    _w = jnp.asarray

    def _rec_inputs():
        import jax
        import jax.numpy as jnp
        _gk = jax.random.key(seed)
        x = -0.000929 + 1 * jax.random.normal(jax.random.fold_in(_gk, 1), (8, 2048, 64), jnp.float32)
        _w = (1.0 + jnp.arange(2048, dtype=jnp.float32)) ** (-0.5)
        _w = _w / _w.mean()
        _pij = jnp.clip(0.00390625 * _w[:, None] * _w[None, :], 0.0, 1.0)
        _a = jax.random.uniform(jax.random.fold_in(_gk, 2), (8, 2048, 2048)) < _pij
        _a = jnp.logical_or(_a, jnp.eye(2048, dtype=bool))
        _af = _a.astype(jnp.float32)
        _af = _af * jax.random.uniform(jax.random.fold_in(_gk, 3), (8, 2048, 2048), jnp.float32, 0.05, 1)
        adj = _af
        return (x, adj)
    x, adj = _rec_inputs()

    def _L0_gnn_setup():
        import jax, jax.numpy as jnp
        import numpy as np
        B, N, C, R = (4, 2048, 64, 16)
        EPS = 1e-12
        key = jax.random.key(seed)
        k_x, k_w, k_u = jax.random.split(key, 3)
        x = jax.random.normal(k_x, (B, N, C), dtype=jnp.float32)
        W = jax.random.uniform(k_w, (B, N, N), dtype=jnp.float32)
        U = 0.01 * jax.random.normal(k_u, (N, R), dtype=jnp.float32)
        w_scale = jnp.asarray(1.0, dtype=jnp.float32)
        return {'x': x, 'W': W, 'U': U, 'w_scale': w_scale}
    _L0_gnn_all = _L0_gnn_setup()
    _L0_gnn_in = {k: v for k, v in _L0_gnn_all.items() if k in ('U', 'w_scale')}
    del _L0_gnn_all
    return {'x': x, 'adj': adj, 'L0_gnn_U': _L0_gnn_in['U'], 'L0_gnn_w_scale': _L0_gnn_in['w_scale']}

def reference(x, adj, L0_gnn_U, L0_gnn_w_scale):
    import jax
    import jax.numpy as jnp

    def _L0_gnn_ref(x, W, U, w_scale):
        import jax, jax.numpy as jnp
        import numpy as np
        B, N, C, R = (4, 2048, 64, 16)
        EPS = 1e-12
        Ws = 0.5 * (W + jnp.swapaxes(W, -1, -2))
        A = jax.nn.sigmoid(U @ U.T)
        K = Ws * A[None, :, :]
        deg = jnp.maximum(K.sum(axis=-1), EPS)
        d = jax.lax.rsqrt(deg)
        K = K * d[:, :, None] * d[:, None, :]
        return w_scale * jnp.einsum('bnm,bmc->bnc', K, x)
    x = _layernorm(x + _L0_gnn_ref(x, adj, L0_gnn_U, L0_gnn_w_scale), axis=-1)
    return x

_drawn_inputs = setup_inputs


def setup_inputs(seed=0):
    import zlib

    import numpy as np

    out = dict(_drawn_inputs(seed))
    spreads = {}
    factors = {'L0_gnn_U': 64.0}
    for name, (base, spread) in spreads.items():
        noise = np.random.default_rng([zlib.crc32(name.encode()), seed]).standard_normal(out[name].shape)
        drawn = base * np.exp(spread * noise) if base else spread * noise
        out[name] = jnp.asarray(drawn.astype(out[name].dtype))
    for name, factor in factors.items():
        out[name] = (out[name] * factor).astype(out[name].dtype)
    return out
```

```python
from contextlib import ExitStack

import numpy as np

import concourse.bass as bass
from concourse import mybir

ALU = mybir.AluOpType
ACT = mybir.ActivationFunctionType
F32 = mybir.dt.float32
F32R = mybir.dt.float32r
AX_X = mybir.AxisListType.X

P = 128
G = 4
UW = G * P
DEG_EPS = 1e-12
LN_EPS = 1e-5

STEPS = [(1, 0), (1, 1), (0, 0), (2, 0), (3, 1), (3, 0), (2, 1), (3, 2), (2, 2), (3, 3)]
HALF0_STEP = 6
LOADS = [u for i, j in STEPS for u in (((i, j), (j, i)) if i != j else ((i, j),))]

PAIRS = [((1, 0), (0, 1)), ((0, 0), (1, 1)), ((0, 2), (0, 3)), ((1, 2), (1, 3)),
         ((2, 0), (3, 1)), ((3, 0), (2, 1)), ((3, 2), (2, 3)), ((2, 2), (3, 3))]
PAIR_OF = {u: q for q, pair in enumerate(PAIRS) for u in pair}


def lower_width(step, r):
    i, j = STEPS[step]
    return UW if i != j else P * (r + 1)


def upper_rows(step):
    return G if STEPS[step][0] != STEPS[step][1] else G - 1


LOWER = [(s, r) for s in range(len(STEPS)) for r in range(G)]
UPPER = [(s, r) for s in range(len(STEPS)) for r in range(upper_rows(s))]
NL, NU, NQ = len(LOWER), len(UPPER), len(PAIRS)
UPPERS_TO = [sum(upper_rows(t) for t in range(s + 1)) for s in range(len(STEPS))]
A_AT = [sum(lower_width(*g) for g in LOWER[:n]) for n in range(NL + 1)]

CARRIED = range(4, NQ)
CARRIED_PARTS = [4, 4, 3, 3, 2]
OWN_PARTS = {8: 4, 9: 4, 10: 8}
YT_STEP = 5
Y_COPY_STEP = 4


def bass_graph_resnorm_kernel(nc, x, adj, u, w_scale, out):
    B, N, C = x.shape
    R = u.shape[1]
    NC = N // P
    NU_SIDE = N // UW
    assert N == NU_SIDE * UW and 2 * C == P and 4 * R <= P and NU_SIDE == 4

    with ExitStack() as ctx:
        def sb(name, shape, dt=F32, scope=ctx):
            return scope.enter_context(nc.sbuf_tensor(name, shape, dt))

        def sem(name):
            return ctx.enter_context(nc.semaphore(name))

        with ExitStack() as early:
            ut_a = sb("ut_a", [P, N], F32R, early)
            ut_b = sb("ut_b", [P, N], F32R, early)
            stack_a = sb("stack_a", [P, NC, P], F32, early)
            stack_b = sb("stack_b", [P, NC, P], F32, early)
        place = [(2, 2), (3, 3), (3, 2), (2, 3)]
        place += [n for n in LOADS if n not in place]
        K = {n: sb(f"k_{n[0]}{n[1]}", [P, G, UW]) for n in place}
        A = sb("gate", [P, A_AT[NL]])
        xt = sb("xt", [P, NC, C])
        z = sb("z", [P, NC, C])
        h = sb("h", [P, NC, C])
        y_sb = sb("y_sb", [P, 2, UW])
        ident = sb("ident", [P, P])
        deg_parts = sb("deg_parts", [P, NC, 5])
        deg = sb("deg", [P, NC])
        d = sb("d", [P, NC])
        f = sb("f", [P, NC])
        minus_half = sb("minus_half", [P, NC])
        mean = sb("mean", [P, NC])
        var = sb("var", [P, NC])
        rstd = sb("rstd", [P, NC])
        ws = sb("ws", [P, 1])
        u_sb = h[:, :, :].rearrange("p n c -> p (n c)")[:, 0:NC * R].rearrange("p (n r) -> p n r", n=NC)

        tw = ctx.enter_context(nc.psum_tensor("tw", [P, 2, UW], F32))
        kt = ctx.enter_context(nc.psum_tensor("kt", [P, 2, UW], F32))
        yp = ctx.enter_context(nc.psum_tensor("yp", [P, 2, UW], F32))
        yt = ctx.enter_context(nc.psum_tensor("yt", [P, 2, UW], F32))

        loaded = {n: sem(f"loaded_{n[0]}{n[1]}") for n in LOADS}
        u_loaded, ws_loaded, x_loaded, out_stored = sem("u_loaded"), sem("ws_loaded"), sem("x_loaded"), sem("out_stored")
        const_ready, ident_ready = sem("const_ready"), sem("ident_ready")
        high_ready, stack_ready = sem("high_ready"), sem("stack_ready")
        ut_done, ut_copied = sem("ut_done"), sem("ut_copied")
        uu_done, gate_ready = sem("uu_done"), sem("gate_ready")
        tw_done, sum_done, lower_done = sem("tw_done"), sem("sum_done"), sem("lower_done")
        kt_done, upper_done = sem("kt_done"), sem("upper_done")
        deg_summed, deg_ready, d_ready, z_ready = sem("deg_summed"), sem("deg_ready"), sem("d_ready"), sem("z_ready")
        prod_done, y_copied, yt_done = sem("prod_done"), sem("y_copied"), sem("yt_done")
        f_ready, y_scaled, h_ready = sem("f_ready"), sem("y_scaled"), sem("h_ready")
        h_summed, mean_ready, centered, squared = sem("h_summed"), sem("mean_ready"), sem("centered"), sem("squared")
        sq_summed, var_ready, rstd_ready, normed = sem("sq_summed"), sem("var_ready"), sem("rstd_ready"), sem("normed")

        first_unit = {m: min(q for q, pair in enumerate(PAIRS) for n in pair if n[1] == m) for m in range(NU_SIDE)}
        last_unit = {m: max(q for q, pair in enumerate(PAIRS) for n in pair if n[1] == m) for m in range(NU_SIDE)}

        def rows_of(t, b):
            return t[b, :, :].rearrange("(n p) c -> p n c", p=P)

        def per_row(v, n0, n1):
            return v[:, n0:n1].unsqueeze(2).broadcast_to([P, n1 - n0, C])

        block = ctx.enter_context(nc.Block())

        @block.sync
        def _(sp):
            def load_unit(b, n):
                i, j = n
                src = adj[b, i * UW:(i + 1) * UW, j * UW:(j + 1) * UW].rearrange("(g p) m -> p g m", p=P)
                sp.dma_start(K[n][:, :, :], src).then_inc(loaded[n], 16)

            sp.dma_start(u_sb, u.rearrange("(n p) r -> p n r", p=P)).then_inc(u_loaded, 16)
            for n in LOADS:
                if n in ((3, 2), (2, 3)):
                    sp.wait_ge(ut_done, 8)
                if n in ((2, 2), (3, 3)):
                    sp.wait_ge(uu_done, NL)
                load_unit(0, n)
            with sp.Fori(1, B) as b:
                passed = -1
                for n in LOADS:
                    if PAIR_OF[n] > passed:
                        passed = PAIR_OF[n]
                        sp.wait_ge(prod_done, b * NQ + (passed + 1 - NQ))
                    load_unit(b, n)
                sp.wait_ge(normed, b)
                sp.dma_start(rows_of(out, b - 1), h[:, :, :]).then_inc(out_stored, 16)
            sp.wait_ge(normed, B)
            sp.dma_start(rows_of(out, B - 1), h[:, :, :]).then_inc(out_stored, 16)
            sp.wait_ge(out_stored, 16 * B)

        @block.gpsimd
        def _(pool):
            nc.gpsimd.memset(ident[:, :], 0.0).then_inc(const_ready, 1)
            pool.wait_ge(const_ready, 1)
            nc.gpsimd.affine_select(out=ident[:, :], in_=ident[:, :], compare_op=ALU.not_equal, fill=1.0,
                                    base=0, pattern=[[-1, P]], channel_multiplier=1).then_inc(ident_ready, 1)
            nc.gpsimd.memset(minus_half[:, :], -0.5).then_inc(const_ready, 1)
            pool.wait_ge(const_ready, 2)

            def norm(b):
                pool.wait_ge(y_scaled, 2 * b + 2)
                nc.gpsimd.tensor_tensor(h[:, :, :], h[:, :, :], xt[:, :, :], ALU.add).then_inc(h_ready, 1)
                pool.wait_ge(mean_ready, b + 1)
                nc.gpsimd.tensor_tensor(h[:, :, :], h[:, :, :], per_row(mean, 0, NC),
                                        ALU.add).then_inc(centered, 1)
                pool.wait_ge(var_ready, b + 1)
                nc.gpsimd.tensor_tensor(rstd[:, :], var[:, :], minus_half[:, :], ALU.pow).then_inc(rstd_ready, 1)
                pool.wait_ge(rstd_ready, b + 1)
                nc.gpsimd.tensor_tensor(h[:, :, :], h[:, :, :], per_row(rstd, 0, NC),
                                        ALU.mult).then_inc(normed, 1)

            def degrees(b, half):
                pool.wait_ge(deg_ready, 2 * b + half + 1)
                s = slice(8 * half, 8 * half + 8)
                nc.gpsimd.tensor_tensor(d[:, s], deg[:, s], minus_half[:, s], ALU.pow).then_inc(d_ready, 1)

            degrees(0, 0)
            degrees(0, 1)
            with pool.Fori(1, B) as b:
                norm(b - 1)
                degrees(b, 0)
                degrees(b, 1)
            norm(B - 1)

        @block.tensor
        def _(pe):
            def transpose_adjacency(b, s, r, first):
                i, j = STEPS[s]
                g = s * G + r
                if r == 0:
                    pe.wait_ge(loaded[(j, i)], b * 16 + 16)
                if not (first and g < 2):
                    pe.wait_ge(sum_done, b * NL + (g - 1))
                for c in range(lower_width(s, r) // P):
                    t = pe.transpose(tw[:, g % 2, c * P:(c + 1) * P], K[(j, i)][:, c, r * P:(r + 1) * P],
                                     ident[:, :])
                t.then_inc(tw_done, 1)

            def transpose_rows(b, s, r, first):
                i, j = STEPS[s]
                g = UPPER.index((s, r))
                if r == 0:
                    pe.wait_ge(lower_done, b * NL + G * (s + 1))
                if not (first and g < 2):
                    pe.wait_ge(upper_done, b * NU + (g - 1))
                chunks = range(G) if i != j else range(r + 1, G)
                for k, c in enumerate(chunks):
                    t = pe.transpose(kt[:, g % 2, k * P:(k + 1) * P], K[(i, j)][:, c, r * P:(r + 1) * P],
                                     ident[:, :])
                t.then_inc(kt_done, 1)

            def product(b, q, c, first=False):
                if c == 0:
                    half = max(n[0] for n in PAIRS[q]) // 2
                    if q in (0, 4):
                        pe.wait_ge(z_ready, 2 * b + half + 1)
                    if q == 0 and not first:
                        pe.wait_ge(y_copied, 2 * b)
                for n, m in PAIRS[q]:
                    at = (m % 2) * C
                    t = pe.matmul(yp[at:at + C, m // 2, :], z[:, n * G + c, :], K[(n, m)][:, c, :],
                                  start=(q == first_unit[m] and c == 0), stop=(q == last_unit[m] and c == G - 1))
                if c == G - 1:
                    t.then_inc(prod_done, 1)

            def transpose_y(b, first):
                for k in range(2):
                    pe.wait_ge(y_copied, 2 * b + (k + 1))
                    if k == 0 and not first:
                        pe.wait_ge(y_scaled, 2 * b)
                    for c in range(G):
                        t = pe.transpose(yt[:, k, c * P:(c + 1) * P], y_sb[:, k, c * P:(c + 1) * P], ident[:, :])
                    t.then_inc(yt_done, 1)

            def outer_product(g):
                s, r = LOWER[g]
                i, j = STEPS[s]
                if g >= 2:
                    pe.wait_ge(gate_ready, g - 1)
                w = lower_width(s, r)
                pe.matmul(yt[:, g % 2, 0:w], ut_a[:, (i * G + r) * P:(i * G + r + 1) * P],
                          ut_b[:, j * UW:j * UW + w], start=True, stop=True).then_inc(uu_done, 1)

            def steps(b, first):
                carried = [(q, c) for q in CARRIED for c in range(G)]
                own = [(q, c) for q in range(NQ) if q not in CARRIED for c in range(G)]
                for s in range(len(STEPS) + 1):
                    parts = []
                    if s < len(CARRIED_PARTS) and not first:
                        parts = [(b - 1, *p) for p in carried[:CARRIED_PARTS[s]]]
                        carried = carried[CARRIED_PARTS[s]:]
                    elif s in OWN_PARTS:
                        parts = [(b, *p) for p in own[:OWN_PARTS[s]]]
                        own = own[OWN_PARTS[s]:]
                    if first and s < 8:
                        for g in range(5 * s, 5 * s + 5):
                            outer_product(g)
                    if s == YT_STEP and not first:
                        transpose_y(b - 1, False)
                    ups = upper_rows(s - 1) if s else 0
                    for r in range(G + 1):
                        if r < G and s < len(STEPS):
                            transpose_adjacency(b, s, r, first)
                        for part in parts[r * len(parts) // G:(r + 1) * len(parts) // G]:
                            product(*part, first=first)
                        if s and 1 <= r <= ups:
                            transpose_rows(b, s - 1, r - 1, first)

            pe.wait_ge(ident_ready, 1)
            for k, (src, dst) in enumerate([(stack_a, yp), (stack_a, yt), (stack_b, tw), (stack_b, kt)]):
                if k % 2 == 0:
                    pe.wait_ge(stack_ready, k // 2 + 1)
                for n in range(8):
                    t = pe.transpose(dst[:, n // G, (n % G) * P:(n % G + 1) * P], src[:, 8 * (k % 2) + n, :],
                                     ident[:, :])
                    if n % G == G - 1:
                        t.then_inc(ut_done, 1)
            pe.wait_ge(ut_copied, 8)
            steps(0, True)
            with pe.Fori(1, B) as b:
                steps(b, False)
            for q in CARRIED:
                for c in range(G):
                    product(B - 1, q, c)
            transpose_y(B - 1, False)

        @block.scalar
        def _(act):
            def gate_row(g):
                w = lower_width(*LOWER[g])
                act.wait_ge(uu_done, g + 1)
                nc.scalar.activation(A[:, A_AT[g]:A_AT[g] + w], yt[:, g % 2, 0:w],
                                     ACT.Sigmoid).then_inc(gate_ready, 1)

            def upper_row(b, s, r):
                i, j = STEPS[s]
                g = UPPER.index((s, r))
                c0, part = (0, i) if i != j else (P * (r + 1), 4)
                n = j * G + r
                act.wait_ge(kt_done, b * NU + (g + 1))
                nc.scalar.activation(K[(j, i)][:, r, c0:UW], kt[:, g % 2, 0:UW - c0], ACT.Copy,
                                     accum_out=deg_parts[:, n, part:part + 1]).then_inc(upper_done, 1)

            def copy_y(b):
                act.wait_ge(prod_done, b * NQ + NQ)
                for k in range(2):
                    nc.scalar.activation(y_sb[:, k, :], yp[:, k, :], ACT.Copy).then_inc(y_copied, 1)

            def square(b):
                act.wait_ge(centered, b + 1)
                nc.scalar.activation(y_sb[:, :, :].rearrange("p k w -> p (k w)"),
                                     h[:, :, :].rearrange("p n c -> p (n c)"), ACT.Square).then_inc(squared, 1)

            def load_x(b):
                act.dma_start(xt[:, :, :], rows_of(x, b)).then_inc(x_loaded, 16)

            def steps(b, first):
                for s in range(len(STEPS) + 1):
                    if first and s < 8:
                        for g in range(5 * s, 5 * s + 5):
                            gate_row(g)
                    for r in range(upper_rows(s - 1) if s else 0):
                        upper_row(b, s - 1, r)
                    if first:
                        continue
                    if s == Y_COPY_STEP:
                        act.wait_ge(sq_summed, b - 1) if False else None
                        copy_y(b - 1)
                    if s == 6:
                        act.wait_ge(h_ready, b)
                        load_x(b)
                    if s == 7:
                        square(b - 1)

            act.dma_start(ws[:, :], w_scale.partition_broadcast(P)).then_inc(ws_loaded, 16)
            load_x(0)
            act.wait_ge(ut_done, 8)
            for k in range(4):
                src = (tw, kt)[k // 2]
                nc.scalar.activation(ut_b[:, k * UW:(k + 1) * UW], src[:, k % 2, :], ACT.Copy).then_inc(ut_copied, 1)
            steps(0, True)
            with act.Fori(1, B) as b:
                steps(b, False)
            copy_y(B - 1)
            square(B - 1)

        @block.vector
        def _(dve):
            def add_row(b, g):
                s, r = LOWER[g]
                w = lower_width(s, r)
                row = K[STEPS[s]][:, r, 0:w]
                if r == 0:
                    dve.wait_ge(loaded[STEPS[s]], b * 16 + 16)
                dve.wait_ge(tw_done, b * NL + (g + 1))
                nc.vector.tensor_tensor(row, tw[:, g % 2, 0:w], row, ALU.add).then_inc(sum_done, 1)

            def gate_product(b, g, first):
                s, r = LOWER[g]
                i, j = STEPS[s]
                w = lower_width(s, r)
                row = K[(i, j)][:, r, 0:w]
                if first:
                    dve.wait_ge(gate_ready, g + 1)
                dve.wait_ge(sum_done, b * NL + (g + 1))
                nc.vector.tensor_tensor_reduce(row, row, A[:, A_AT[g]:A_AT[g] + w], 1.0, 0.0, ALU.mult, ALU.add,
                                               deg_parts[:, i * G + r, j:j + 1]).then_inc(lower_done, 1)

            def make_z(b, half, first):
                n0, n1 = 8 * half, 8 * half + 8
                top = len(STEPS) - 1 if half else HALF0_STEP
                dve.wait_ge(lower_done, b * NL + G * (top + 1))
                dve.wait_ge(upper_done, b * NU + UPPERS_TO[top])
                nc.vector.tensor_reduce(deg[:, n0:n1], deg_parts[:, n0:n1, :], AX_X, ALU.add).then_inc(deg_summed, 1)
                dve.wait_ge(deg_summed, 2 * b + (half + 1))
                nc.vector.tensor_scalar(deg[:, n0:n1], deg[:, n0:n1], 0.5, DEG_EPS, ALU.mult,
                                        ALU.max).then_inc(deg_ready, 1)
                dve.wait_ge(d_ready, 2 * b + (half + 1))
                dve.wait_ge(x_loaded, b * 16 + 16)
                if not first:
                    dve.wait_ge(prod_done, b * NQ)
                nc.vector.tensor_tensor(z[:, n0:n1, :], xt[:, n0:n1, :], per_row(d, n0, n1),
                                        ALU.mult).then_inc(z_ready, 1)

            def scale_y(b, first):
                nc.vector.tensor_scalar(f[:, :], d[:, :], ws[:, 0:1], 0.5, ALU.mult, ALU.mult).then_inc(f_ready, 1)
                dve.wait_ge(f_ready, b + 1)
                if not first:
                    dve.wait_ge(out_stored, b * 16)
                for k in range(2):
                    dve.wait_ge(yt_done, 2 * b + (k + 1))
                    src = yt[:, k, :].rearrange("p (c half e) -> p half c e", c=G, half=2)
                    fk = f[:, 8 * k:8 * k + 8].rearrange("p (half c) -> p half c", half=2).unsqueeze(3)
                    dst = h[:, 8 * k:8 * k + 8, :].rearrange("p (half c) e -> p half c e", half=2)
                    nc.vector.tensor_tensor(dst, src, fk.broadcast_to([P, 2, G, C]),
                                            ALU.mult).then_inc(y_scaled, 1)

            def row_mean(b):
                dve.wait_ge(h_ready, b + 1)
                nc.vector.tensor_reduce(mean[:, :], h[:, :, :], AX_X, ALU.add).then_inc(h_summed, 1)
                dve.wait_ge(h_summed, b + 1)
                nc.vector.tensor_scalar(mean[:, :], mean[:, :], -1.0 / C, None, ALU.mult).then_inc(mean_ready, 1)

            def row_var(b):
                dve.wait_ge(squared, b + 1)
                nc.vector.tensor_reduce(var[:, :], y_sb[:, :, :].rearrange("p k (n c) -> p (k n) c", c=C), AX_X,
                                        ALU.add).then_inc(sq_summed, 1)
                dve.wait_ge(sq_summed, b + 1)
                nc.vector.tensor_scalar(var[:, :], var[:, :], 1.0 / C, LN_EPS, ALU.mult,
                                        ALU.add).then_inc(var_ready, 1)

            def steps(b, first):
                for g in range(NL + 1):
                    if g < NL:
                        add_row(b, g)
                    if g:
                        gate_product(b, g - 1, first)
                    if g == G * 6 and not first:
                        scale_y(b - 1, False)
                    if g == G * 7 and not first:
                        row_mean(b - 1)
                    if g == G * 8 - 2 and not first:
                        row_var(b - 1)
                    if g == G * 8:
                        make_z(b, 0, first)
                make_z(b, 1, first)

            nc.vector.memset(deg_parts[:, :, :], 0.0)
            nc.vector.memset(stack_a[:, :, 4 * R:P], 0.0)
            nc.vector.memset(stack_b[:, :, 4 * R:P], 0.0)
            dve.wait_ge(u_loaded, 16)
            for part, t in ((0, stack_a), (2, stack_a), (0, stack_b), (1, stack_b)):
                last = nc.vector.tensor_copy(t[:, :, part * R:(part + 1) * R].bitcast(F32R), u_sb)
            last.then_inc(high_ready, 1)
            dve.wait_ge(high_ready, 1)
            high = stack_a[:, :, 0:R]
            for t, parts in ((stack_a, (1, 3)), (stack_b, (2, 3))):
                for part in parts:
                    last = nc.vector.tensor_tensor(t[:, :, part * R:(part + 1) * R], u_sb, high, ALU.subtract)
                last.then_inc(stack_ready, 1)
            for k in range(4):
                dve.wait_ge(ut_done, k + 1)
                nc.vector.tensor_copy(ut_a[:, k * UW:(k + 1) * UW], (yp, yt)[k // 2][:, k % 2, :]).then_inc(ut_copied, 1)
            dve.wait_ge(ws_loaded, 16)
            steps(0, True)
            with dve.Fori(1, B) as b:
                steps(b, False)
            scale_y(B - 1, False)
            row_mean(B - 1)
            row_var(B - 1)


_INS = ["x", "adj", "L0_gnn_U", "L0_gnn_w_scale"]


def kernel(**inputs):
    import concourse.bacc as bacc
    from concourse.bass_utils import run_bass_kernel_spmd

    nc = bacc.Bacc("TRN2", target_bir_lowering=False, num_devices=1, dynamic_dma_scratch_size=4096)
    arrays, args = {}, []
    for name in _INS:
        a = np.ascontiguousarray(inputs[name])
        if a.ndim == 0:
            a = a.reshape(1)
        arrays[f"in_{name}_dram"] = a
        args.append(nc.dram_tensor(f"in_{name}_dram", a.shape, mybir.dt.from_np(a.dtype), kind="ExternalInput").ap())
    shape = inputs["x"].shape
    args.append(nc.dram_tensor("out_dram", shape, mybir.dt.from_np(np.dtype("float32")), kind="ExternalOutput").ap())
    bass_graph_resnorm_kernel(nc, *args)
    result = run_bass_kernel_spmd(nc, [arrays], core_ids=[0])
    return result.results[0]["out_dram"]
```

```python
from contextlib import ExitStack

import numpy as np

import concourse.bass as bass
from concourse import mybir

ALU = mybir.AluOpType
ACT = mybir.ActivationFunctionType
F32 = mybir.dt.float32
F32R = mybir.dt.float32r
AX_X = mybir.AxisListType.X

P = 128
G = 4
UW = G * P
DEG_EPS = 1e-12
LN_EPS = 1e-5

STEPS = [(1, 0), (1, 1), (0, 0), (2, 0), (3, 1), (3, 0), (2, 1), (3, 2), (2, 2), (3, 3)]
HALF0_STEP = 6
LOADS = [u for i, j in STEPS for u in (((i, j), (j, i)) if i != j else ((i, j),))]

PAIRS = [((1, 0), (0, 1)), ((0, 0), (1, 1)), ((0, 2), (0, 3)), ((1, 2), (1, 3)),
         ((2, 0), (3, 1)), ((3, 0), (2, 1)), ((3, 2), (2, 3)), ((2, 2), (3, 3))]
PAIR_OF = {u: q for q, pair in enumerate(PAIRS) for u in pair}


def lower_width(step, r):
    i, j = STEPS[step]
    return UW if i != j else P * (r + 1)


def upper_rows(step):
    return G if STEPS[step][0] != STEPS[step][1] else G - 1


LOWER = [(s, r) for s in range(len(STEPS)) for r in range(G)]
UPPER = [(s, r) for s in range(len(STEPS)) for r in range(upper_rows(s))]
NL, NU, NQ = len(LOWER), len(UPPER), len(PAIRS)
RING = 3
UPPERS_TO = [sum(upper_rows(t) for t in range(s + 1)) for s in range(len(STEPS))]
A_AT = [sum(lower_width(*g) for g in LOWER[:n]) for n in range(NL + 1)]

OWN = 2
CARRIED_PARTS = [10, 4, 2, 2, 1, 2, 3, 0]
OWN_PARTS = [0] * 9 + [3, 5]
LAST_CARRIED_STEP = len(CARRIED_PARTS) - 1
STORE_AFTER = 16
UPPER_LAG = 2

Y_AT, KEEP_AT, MEAN_AT, SQUARE_AT, VAR_AT, COPY_AT, DEG0_AT, Z0_AT = 0, 5, 6, 5, 12, 33, 33, 34


def bass_graph_resnorm_kernel(nc, x, adj, u, w_scale, out):
    B, N, C = x.shape
    R = u.shape[1]
    NC = N // P
    NU_SIDE = N // UW
    assert N == NU_SIDE * UW and 2 * C == P and 4 * R <= P and NU_SIDE == 4

    with ExitStack() as ctx:
        def sb(name, shape, dt=F32, scope=ctx):
            return scope.enter_context(nc.sbuf_tensor(name, shape, dt))

        def sem(name):
            return ctx.enter_context(nc.semaphore(name))

        with ExitStack() as early:
            ut_a = sb("ut_a", [P, N], F32R, early)
            ut_b = sb("ut_b", [P, N], F32R, early)
            stack_a = sb("stack_a", [P, NC, P], F32, early)
            stack_b = sb("stack_b", [P, NC, P], F32, early)
        place = [(2, 2), (3, 3), (3, 2), (2, 3)]
        place += [n for n in LOADS if n not in place]
        K = {n: sb(f"k_{n[0]}{n[1]}", [P, G, UW]) for n in place}
        A = sb("gate", [P, A_AT[NL]])
        xt = sb("xt", [P, NC, C])
        x_keep = sb("x_keep", [P, NC, C])
        z = sb("z", [P, NC, C])
        h = sb("h", [P, NC, C])
        y_sb = sb("y_sb", [P, 2, UW])
        ident = sb("ident", [P, P])
        deg_parts = sb("deg_parts", [P, NC, 5])
        deg = sb("deg", [P, NC])
        d = sb("d", [P, NC])
        f = sb("f", [P, NC])
        minus_half = sb("minus_half", [P, NC])
        mean = sb("mean", [P, NC])
        var = sb("var", [P, NC])
        rstd = sb("rstd", [P, NC])
        ws = sb("ws", [P, 1])
        u_sb = h[:, :, :].rearrange("p n c -> p (n c)")[:, 0:NC * R].rearrange("p (n r) -> p n r", n=NC)

        tw = ctx.enter_context(nc.psum_tensor("tw", [P, RING, UW], F32))
        kt = ctx.enter_context(nc.psum_tensor("kt", [P, RING, UW], F32))
        yp = ctx.enter_context(nc.psum_tensor("yp", [P, 2, UW], F32))
        y_bank = [(Y_AT + k) % RING for k in range(2)]

        def tw_bank(g):
            return (g if g < Y_AT else g + 2) % RING

        loaded = {n: sem(f"loaded_{n[0]}{n[1]}") for n in LOADS}
        h_moved, ws_loaded, x_loaded = sem("h_moved"), sem("ws_loaded"), sem("x_loaded")
        x_kept = sem("x_kept")
        const_ready, ident_ready = sem("const_ready"), sem("ident_ready")
        high_ready, stack_ready = sem("high_ready"), sem("stack_ready")
        ut_done, ut_copied = sem("ut_done"), sem("ut_copied")
        uu_done, gate_ready = sem("uu_done"), sem("gate_ready")
        tw_done, sum_done, lower_done = sem("tw_done"), sem("sum_done"), sem("lower_done")
        kt_done, upper_done = sem("kt_done"), sem("upper_done")
        deg_summed, deg_ready, d_ready, z_ready = sem("deg_summed"), sem("deg_ready"), sem("d_ready"), sem("z_ready")
        prod_done, y_copied, yt_done = sem("prod_done"), sem("y_copied"), sem("yt_done")
        f_ready, y_scaled, h_ready = sem("f_ready"), sem("y_scaled"), sem("h_ready")
        h_summed, mean_ready, centered, squared = sem("h_summed"), sem("mean_ready"), sem("centered"), sem("squared")
        sq_summed, var_ready, rstd_ready, normed = sem("sq_summed"), sem("var_ready"), sem("rstd_ready"), sem("normed")

        UT_BANKS = [(yp, 0), (yp, 1), (tw, 0), (tw, 1), (tw, 2), (kt, 0), (kt, 1), (kt, 2)]
        first_unit = {m: min(q for q, pair in enumerate(PAIRS) for n in pair if n[1] == m) for m in range(NU_SIDE)}
        last_unit = {m: max(q for q, pair in enumerate(PAIRS) for n in pair if n[1] == m) for m in range(NU_SIDE)}

        def rows_of(t, b):
            return t[b, :, :].rearrange("(n p) c -> p n c", p=P)

        def per_row(v, n0, n1):
            return v[:, n0:n1].unsqueeze(2).broadcast_to([P, n1 - n0, C])

        block = ctx.enter_context(nc.Block())

        @block.sync
        def _(sp):
            def load_unit(b, n):
                i, j = n
                src = adj[b, i * UW:(i + 1) * UW, j * UW:(j + 1) * UW].rearrange("(g p) m -> p g m", p=P)
                sp.dma_start(K[n][:, :, :], src).then_inc(loaded[n], 16)

            sp.dma_start(u_sb, u.rearrange("(n p) r -> p n r", p=P)).then_inc(h_moved, 16)
            for n in LOADS:
                if n in ((3, 2), (2, 3)):
                    sp.wait_ge(ut_done, 8)
                if n in ((2, 2), (3, 3)):
                    sp.wait_ge(uu_done, NL)
                load_unit(0, n)

            def load_units(b, units):
                passed = -1
                for n in units:
                    if PAIR_OF[n] > passed:
                        passed = PAIR_OF[n]
                        sp.wait_ge(prod_done, b * NQ + (passed + 1 - NQ))
                    load_unit(b, n)

            def store(b):
                sp.wait_ge(normed, b + 1)
                sp.dma_start(rows_of(out, b), h[:, :, :]).then_inc(h_moved, 16)

            load_units(1, LOADS)
            with sp.Fori(2, B) as b:
                load_units(b, LOADS[:STORE_AFTER])
                store(b - 2)
                if STORE_AFTER < len(LOADS):
                    load_units(b, LOADS[STORE_AFTER:])
            store(B - 2)
            store(B - 1)
            sp.wait_ge(h_moved, 16 * (B + 1))

        @block.gpsimd
        def _(pool):
            nc.gpsimd.memset(ident[:, :], 0.0).then_inc(const_ready, 1)
            pool.wait_ge(const_ready, 1)
            nc.gpsimd.affine_select(out=ident[:, :], in_=ident[:, :], compare_op=ALU.not_equal, fill=1.0,
                                    base=0, pattern=[[-1, P]], channel_multiplier=1).then_inc(ident_ready, 1)
            nc.gpsimd.memset(minus_half[:, :], -0.5).then_inc(const_ready, 1)
            pool.wait_ge(const_ready, 2)

            def add_x(b):
                pool.wait_ge(y_scaled, 2 * b + 2)
                pool.wait_ge(x_kept, b + 1)
                nc.gpsimd.tensor_tensor(h[:, :, :], h[:, :, :], x_keep[:, :, :], ALU.add).then_inc(h_ready, 1)

            def center(b):
                pool.wait_ge(mean_ready, b + 1)
                nc.gpsimd.tensor_tensor(h[:, :, :], h[:, :, :], per_row(mean, 0, NC),
                                        ALU.add).then_inc(centered, 1)

            def divide(b):
                pool.wait_ge(var_ready, b + 1)
                nc.gpsimd.tensor_tensor(rstd[:, :], var[:, :], minus_half[:, :], ALU.pow).then_inc(rstd_ready, 1)
                pool.wait_ge(rstd_ready, b + 1)
                nc.gpsimd.tensor_tensor(h[:, :, :], h[:, :, :], per_row(rstd, 0, NC),
                                        ALU.mult).then_inc(normed, 1)

            def degrees(b, half):
                pool.wait_ge(deg_ready, 2 * b + half + 1)
                s = slice(8 * half, 8 * half + 8)
                nc.gpsimd.tensor_tensor(d[:, s], deg[:, s], minus_half[:, s], ALU.pow).then_inc(d_ready, 1)

            def finish(b):
                add_x(b)
                center(b)
                divide(b)

            for b in range(2):
                degrees(b, 0)
                degrees(b, 1)
            with pool.Fori(2, B) as b:
                finish(b - 2)
                degrees(b, 0)
                degrees(b, 1)
            finish(B - 2)
            finish(B - 1)

        @block.tensor
        def _(pe):
            def bank_free(b, place, stage):
                before = place - RING
                if before in (Y_AT, Y_AT + 1):
                    if stage == 2:
                        pe.wait_ge(y_scaled, 2 * b + (before - Y_AT - 3))
                elif before >= 0 or stage:
                    pe.wait_ge(sum_done, b * NL + (before + 1 if before < Y_AT else before - 1))

            def transpose_adjacency(b, s, r, stage):
                i, j = STEPS[s]
                g = s * G + r
                if r == 0:
                    pe.wait_ge(loaded[(j, i)], b * 16 + 16)
                bank_free(b, g if g < Y_AT else g + 2, stage)
                for c in range(lower_width(s, r) // P):
                    t = pe.transpose(tw[:, tw_bank(g), c * P:(c + 1) * P], K[(j, i)][:, c, r * P:(r + 1) * P],
                                     ident[:, :])
                t.then_inc(tw_done, 1)

            def transpose_rows(b, s, r, stage):
                i, j = STEPS[s]
                g = UPPER.index((s, r))
                if r == 0:
                    pe.wait_ge(lower_done, b * NL + G * (s + 1))
                if stage or g >= RING:
                    pe.wait_ge(upper_done, b * NU + (g + 1 - RING))
                chunks = range(G) if i != j else range(r + 1, G)
                for k, c in enumerate(chunks):
                    t = pe.transpose(kt[:, g % RING, k * P:(k + 1) * P], K[(i, j)][:, c, r * P:(r + 1) * P],
                                     ident[:, :])
                t.then_inc(kt_done, 1)

            def product(b, q, c, stage=2):
                if c == 0:
                    if q in (0, 4):
                        pe.wait_ge(z_ready, 2 * b + q // 4 + 1)
                    if q == 0 and stage == 0:
                        pe.wait_ge(gate_ready, NL)
                    elif q == 0:
                        pe.wait_ge(y_copied, 2 * b)
                for n, m in PAIRS[q]:
                    at = (m % 2) * C
                    t = pe.matmul(yp[at:at + C, m // 2, :], z[:, n * G + c, :], K[(n, m)][:, c, :],
                                  start=(q == first_unit[m] and c == 0), stop=(q == last_unit[m] and c == G - 1))
                if c == G - 1:
                    t.then_inc(prod_done, 1)

            def transpose_y(b, ending=False):
                for k in range(2):
                    pe.wait_ge(y_copied, 2 * b + (k + 1))
                    if not ending:
                        bank_free(b + 2, Y_AT + k, 2)
                    elif k == 0:
                        pe.wait_ge(sum_done, B * NL)
                        pe.wait_ge(y_scaled, 2 * b)
                    for c in range(G):
                        t = pe.transpose(tw[:, y_bank[k], c * P:(c + 1) * P], y_sb[:, k, c * P:(c + 1) * P], ident[:, :])
                    t.then_inc(yt_done, 1)

            def outer_product(g):
                s, r = LOWER[g]
                i, j = STEPS[s]
                if g >= 2:
                    pe.wait_ge(gate_ready, g - 1)
                w = lower_width(s, r)
                pe.matmul(yp[:, g % 2, 0:w], ut_a[:, (i * G + r) * P:(i * G + r + 1) * P],
                          ut_b[:, j * UW:j * UW + w], start=True, stop=True).then_inc(uu_done, 1)

            def steps(b, stage):
                carried = [(b - 1, q, c) for q in range(OWN, NQ) for c in range(G)]
                own = [(b, q, c) for q in range(OWN) for c in range(G)]
                for s in range(len(STEPS) + 1):
                    parts = []
                    if s <= LAST_CARRIED_STEP and stage:
                        at = sum(CARRIED_PARTS[:s])
                        parts += carried[at:at + CARRIED_PARTS[s]]
                    at = sum(OWN_PARTS[:s])
                    parts += own[at:at + OWN_PARTS[s]]
                    if stage == 0 and s < 8:
                        for g in range(5 * s, 5 * s + 5):
                            outer_product(g)
                    for r in range(G + 1 if s == len(STEPS) else G):
                        at = s * G + r
                        if at == Y_AT and stage == 2:
                            transpose_y(b - 2)
                        if at < NL:
                            transpose_adjacency(b, s, r, stage)
                        for part in parts[r * len(parts) // G:(r + 1) * len(parts) // G]:
                            product(*part, stage=stage)
                        for up in UPPER:
                            if at == (up[0] + 1) * G + up[1] + UPPER_LAG:
                                transpose_rows(b, *up, stage)

            pe.wait_ge(ident_ready, 1)
            for k, (dst, bank) in enumerate(UT_BANKS):
                if k % G == 0:
                    pe.wait_ge(stack_ready, k // G + 1)
                src = (stack_a, stack_b)[k // G]
                for n in range(G):
                    t = pe.transpose(dst[:, bank, n * P:(n + 1) * P], src[:, G * (k % G) + n, :], ident[:, :])
                t.then_inc(ut_done, 1)
            pe.wait_ge(ut_copied, 8)
            steps(0, 0)
            steps(1, 1)
            with pe.Fori(2, B) as b:
                steps(b, 2)
            transpose_y(B - 2, ending=True)
            for q in range(OWN, NQ):
                for c in range(G):
                    product(B - 1, q, c)
            transpose_y(B - 1, ending=True)

        @block.scalar
        def _(act):
            def gate_row(g):
                w = lower_width(*LOWER[g])
                act.wait_ge(uu_done, g + 1)
                nc.scalar.activation(A[:, A_AT[g]:A_AT[g] + w], yp[:, g % 2, 0:w],
                                     ACT.Sigmoid).then_inc(gate_ready, 1)

            def upper_row(b, s, r):
                i, j = STEPS[s]
                g = UPPER.index((s, r))
                c0, part = (0, i) if i != j else (P * (r + 1), 4)
                n = j * G + r
                act.wait_ge(kt_done, b * NU + (g + 1))
                nc.scalar.activation(K[(j, i)][:, r, c0:UW], kt[:, g % RING, 0:UW - c0], ACT.Copy,
                                     accum_out=deg_parts[:, n, part:part + 1]).then_inc(upper_done, 1)

            def copy_y(b, early=False):
                act.wait_ge(prod_done, b * NQ + NQ)
                if not early:
                    act.wait_ge(sq_summed, b)
                for k in range(2):
                    nc.scalar.activation(y_sb[:, k, :], yp[:, k, :], ACT.Copy).then_inc(y_copied, 1)

            def square(b):
                act.wait_ge(centered, b + 1)
                nc.scalar.activation(y_sb[:, :, :].rearrange("p k w -> p (k w)"),
                                     h[:, :, :].rearrange("p n c -> p (n c)"), ACT.Square).then_inc(squared, 1)

            def keep_x(b, early=False):
                act.wait_ge(x_loaded, b * 16 + 16)
                if not early:
                    act.wait_ge(h_ready, b)
                nc.scalar.activation(x_keep[:, :, :].rearrange("p n c -> p (n c)"),
                                     xt[:, :, :].rearrange("p n c -> p (n c)"), ACT.Copy).then_inc(x_kept, 1)

            def load_x(b):
                act.dma_start(xt[:, :, :], rows_of(x, b)).then_inc(x_loaded, 16)

            def steps(b, stage):
                for at in range(NL + G + 1):
                    if stage == 0 and at % G == 0 and at < 8 * G:
                        for g in range(5 * (at // G), 5 * (at // G) + 5):
                            gate_row(g)
                    for up in UPPER:
                        if at == (up[0] + 1) * G + up[1] + UPPER_LAG:
                            upper_row(b, *up)
                    if at == KEEP_AT and stage:
                        keep_x(b - 1, early=(stage == 1))
                        act.wait_ge(z_ready, 2 * b)
                        act.wait_ge(x_kept, b)
                        load_x(b)
                    if at == SQUARE_AT and stage == 2:
                        square(b - 2)
                    if at == COPY_AT and stage:
                        copy_y(b - 1, early=(stage == 1))

            act.dma_start(ws[:, :], w_scale.partition_broadcast(P)).then_inc(ws_loaded, 16)
            load_x(0)
            act.wait_ge(ut_done, 8)
            for k in range(4):
                src, bank = UT_BANKS[G + k]
                nc.scalar.activation(ut_b[:, k * UW:(k + 1) * UW], src[:, bank, :], ACT.Copy).then_inc(ut_copied, 1)
            steps(0, 0)
            steps(1, 1)
            with act.Fori(2, B) as b:
                steps(b, 2)
            keep_x(B - 1)
            square(B - 2)
            copy_y(B - 1)
            square(B - 1)

        @block.vector
        def _(dve):
            def add_row(b, g):
                s, r = LOWER[g]
                w = lower_width(s, r)
                row = K[STEPS[s]][:, r, 0:w]
                if r == 0:
                    dve.wait_ge(loaded[STEPS[s]], b * 16 + 16)
                dve.wait_ge(tw_done, b * NL + (g + 1))
                nc.vector.tensor_tensor(row, tw[:, tw_bank(g), 0:w], row, ALU.add).then_inc(sum_done, 1)

            def gate_product(b, g, first):
                s, r = LOWER[g]
                i, j = STEPS[s]
                w = lower_width(s, r)
                row = K[(i, j)][:, r, 0:w]
                if first:
                    dve.wait_ge(gate_ready, g + 1)
                dve.wait_ge(sum_done, b * NL + (g + 1))
                nc.vector.tensor_tensor_reduce(row, row, A[:, A_AT[g]:A_AT[g] + w], 1.0, 0.0, ALU.mult, ALU.add,
                                               deg_parts[:, i * G + r, j:j + 1]).then_inc(lower_done, 1)

            def sum_degrees(b, half):
                n0, n1 = 8 * half, 8 * half + 8
                top = len(STEPS) - 1 if half else HALF0_STEP
                dve.wait_ge(lower_done, b * NL + G * (top + 1))
                dve.wait_ge(upper_done, b * NU + UPPERS_TO[top])
                nc.vector.tensor_reduce(deg[:, n0:n1], deg_parts[:, n0:n1, :], AX_X, ALU.add).then_inc(deg_summed, 1)
                dve.wait_ge(deg_summed, 2 * b + (half + 1))
                nc.vector.tensor_scalar(deg[:, n0:n1], deg[:, n0:n1], 0.5, DEG_EPS, ALU.mult,
                                        ALU.max).then_inc(deg_ready, 1)

            def make_z(b, half, first):
                n0, n1 = 8 * half, 8 * half + 8
                dve.wait_ge(d_ready, 2 * b + (half + 1))
                dve.wait_ge(x_loaded, b * 16 + 16)
                if not first:
                    dve.wait_ge(prod_done, b * NQ)
                nc.vector.tensor_tensor(z[:, n0:n1, :], xt[:, n0:n1, :], per_row(d, n0, n1),
                                        ALU.mult).then_inc(z_ready, 1)

            def scale(b):
                dve.wait_ge(d_ready, 2 * b + 2)
                nc.vector.tensor_scalar(f[:, :], d[:, :], ws[:, 0:1], 0.5, ALU.mult, ALU.mult).then_inc(f_ready, 1)

            def scale_y(b):
                dve.wait_ge(f_ready, b + 1)
                dve.wait_ge(h_moved, b * 16 + 16)
                for k in range(2):
                    dve.wait_ge(yt_done, 2 * b + (k + 1))
                    src = tw[:, y_bank[k], :].rearrange("p (c half e) -> p half c e", c=G, half=2)
                    fk = f[:, 8 * k:8 * k + 8].rearrange("p (half c) -> p half c", half=2).unsqueeze(3)
                    dst = h[:, 8 * k:8 * k + 8, :].rearrange("p (half c) e -> p half c e", half=2)
                    nc.vector.tensor_tensor(dst, src, fk.broadcast_to([P, 2, G, C]),
                                            ALU.mult).then_inc(y_scaled, 1)

            def row_mean(b):
                dve.wait_ge(h_ready, b + 1)
                nc.vector.tensor_reduce(mean[:, :], h[:, :, :], AX_X, ALU.add).then_inc(h_summed, 1)
                dve.wait_ge(h_summed, b + 1)
                nc.vector.tensor_scalar(mean[:, :], mean[:, :], -1.0 / C, None, ALU.mult).then_inc(mean_ready, 1)

            def row_var(b):
                dve.wait_ge(squared, b + 1)
                nc.vector.tensor_reduce(var[:, :], y_sb[:, :, :].rearrange("p k (n c) -> p (k n) c", c=C), AX_X,
                                        ALU.add).then_inc(sq_summed, 1)
                dve.wait_ge(sq_summed, b + 1)
                nc.vector.tensor_scalar(var[:, :], var[:, :], 1.0 / C, LN_EPS, ALU.mult,
                                        ALU.add).then_inc(var_ready, 1)

            def steps(b, stage):
                for g in range(NL + 1):
                    if g == Y_AT and stage == 2:
                        scale_y(b - 2)
                    if g < NL:
                        add_row(b, g)
                    if g:
                        gate_product(b, g - 1, stage == 0)
                    if g == MEAN_AT and stage == 2:
                        row_mean(b - 2)
                    if g == VAR_AT and stage == 2:
                        row_var(b - 2)
                    if g == DEG0_AT:
                        if stage:
                            scale(b - 1)
                        sum_degrees(b, 0)
                    if g == Z0_AT:
                        make_z(b, 0, stage == 0)
                sum_degrees(b, 1)
                make_z(b, 1, stage == 0)

            nc.vector.memset(deg_parts[:, :, :], 0.0)
            nc.vector.memset(stack_a[:, :, 4 * R:P], 0.0)
            nc.vector.memset(stack_b[:, :, 4 * R:P], 0.0)
            dve.wait_ge(h_moved, 16)
            for part, t in ((0, stack_a), (2, stack_a), (0, stack_b), (1, stack_b)):
                last = nc.vector.tensor_copy(t[:, :, part * R:(part + 1) * R].bitcast(F32R), u_sb)
            last.then_inc(high_ready, 1)
            dve.wait_ge(high_ready, 1)
            high = stack_a[:, :, 0:R]
            for t, parts in ((stack_a, (1, 3)), (stack_b, (2, 3))):
                for part in parts:
                    last = nc.vector.tensor_tensor(t[:, :, part * R:(part + 1) * R], u_sb, high, ALU.subtract)
                last.then_inc(stack_ready, 1)
            for k in range(4):
                dve.wait_ge(ut_done, k + 1)
                src, bank = UT_BANKS[k]
                nc.vector.tensor_copy(ut_a[:, k * UW:(k + 1) * UW], src[:, bank, :]).then_inc(ut_copied, 1)
            dve.wait_ge(ws_loaded, 16)
            steps(0, 0)
            steps(1, 1)
            with dve.Fori(2, B) as b:
                steps(b, 2)
            scale_y(B - 2)
            row_mean(B - 2)
            row_var(B - 2)
            scale(B - 1)
            scale_y(B - 1)
            row_mean(B - 1)
            row_var(B - 1)


_INS = ["x", "adj", "L0_gnn_U", "L0_gnn_w_scale"]


def kernel(**inputs):
    import concourse.bacc as bacc
    from concourse.bass_utils import run_bass_kernel_spmd

    nc = bacc.Bacc("TRN2", target_bir_lowering=False, num_devices=1, dynamic_dma_scratch_size=4096)
    arrays, args = {}, []
    for name in _INS:
        a = np.ascontiguousarray(inputs[name])
        if a.ndim == 0:
            a = a.reshape(1)
        arrays[f"in_{name}_dram"] = a
        args.append(nc.dram_tensor(f"in_{name}_dram", a.shape, mybir.dt.from_np(a.dtype), kind="ExternalInput").ap())
    shape = inputs["x"].shape
    args.append(nc.dram_tensor("out_dram", shape, mybir.dt.from_np(np.dtype("float32")), kind="ExternalOutput").ap())
    bass_graph_resnorm_kernel(nc, *args)
    result = run_bass_kernel_spmd(nc, [arrays], core_ids=[0])
    return result.results[0]["out_dram"]
```

```python
from contextlib import ExitStack

import numpy as np

import concourse.bass as bass
from concourse import mybir

ALU = mybir.AluOpType
ACT = mybir.ActivationFunctionType
F32 = mybir.dt.float32
F32R = mybir.dt.float32r
AX_X = mybir.AxisListType.X

P = 128
G = 4
UW = G * P
DEG_EPS = 1e-12
LN_EPS = 1e-5

STEPS = [(0, 0), (1, 0), (1, 1), (2, 0), (3, 0), (2, 1), (3, 1), (3, 2), (2, 2), (3, 3)]
FIRST_LOADS = [u for i, j in STEPS for u in (((j, i), (i, j)) if i != j else ((i, j),))]

Z_GROUPS = [(0, G, 4), (G, 2 * G, 6), (2 * G, 4 * G, 9)]
NZ = len(Z_GROUPS)

PAIRS = [((0, 0), (0, 1)), ((0, 2), (0, 3)), ((1, 0), (1, 1)), ((1, 2), (1, 3)),
         ((2, 0), (3, 1)), ((3, 0), (2, 1)), ((3, 2), (2, 3)), ((2, 2), (3, 3))]
PAIR_OF = {u: q for q, pair in enumerate(PAIRS) for u in pair}
Z_OF_PAIR = {0: 0, 2: 1, 4: 2}
LOADS = [(0, 1), (0, 0)] + [u for pair in PAIRS[1:] for u in pair]


def lower_width(step, r):
    i, j = STEPS[step]
    return UW if i != j else P * (r + 1)


def upper_rows(step):
    return G if STEPS[step][0] != STEPS[step][1] else G - 1


LOWER = [(s, r) for s in range(len(STEPS)) for r in range(G)]
UPPER = [(s, r) for s in range(len(STEPS)) for r in range(upper_rows(s))]
NL, NU, NQ = len(LOWER), len(UPPER), len(PAIRS)
RING = 3
UPPERS_TO = [sum(upper_rows(t) for t in range(s + 1)) for s in range(len(STEPS))]
A_AT = [sum(lower_width(*g) for g in LOWER[:n]) for n in range(NL + 1)]

OWN = 4
OWN_ROWS = [28, 28, 30, 31, 32, 33, 34, 36, 38, 39, 39, 40, 45, 45, 45, 45]
FIRST_OWN_ROWS = [28, 29, 30, 31, 32, 33, 34, 35, 36, 38, 39, 40, 45, 45, 45, 45]
CARRIED_ROWS = [2, 4, 4, 5, 7, 8, 10, 11, 13, 15, 17, 18, 18, 21, 22, 24]
UPPER_LAG = 2

Y_AT, KEEP_AT, MEAN_AT, SQUARE_AT, VAR_AT, COPY_AT = 5, 6, 11, 13, 15, 26
DEG0_AT, Z0_AT, DEG1_AT, Z1_AT = 24, 25, 33, 34
FIRST_DEG0_AT, FIRST_Z0_AT, FIRST_DEG1_AT, FIRST_Z1_AT = 24, 25, 32, 33
X_AFTER = 9
GATES = 3


def gates_before(row):
    return min(NL, 1 + GATES * row // 2) if row else 0


LAST_PAIRS = [((2, 0), (2, 1)), ((3, 0), (3, 1)), ((2, 2), (2, 3)), ((3, 2), (3, 3))]
LAST_BANK0 = 2
LAST_Y_CHUNK = 2


def bass_graph_resnorm_kernel(nc, x, adj, u, w_scale, out):
    B, N, C = x.shape
    R = u.shape[1]
    NC = N // P
    NU_SIDE = N // UW
    assert N == NU_SIDE * UW and 2 * C == P and 4 * R <= P and NU_SIDE == 4

    with ExitStack() as ctx:
        def sb(name, shape, dt=F32, scope=ctx):
            return scope.enter_context(nc.sbuf_tensor(name, shape, dt))

        def sem(name):
            return ctx.enter_context(nc.semaphore(name))

        with ExitStack() as early:
            ut_a = sb("ut_a", [P, N], F32R, early)
            ut_b = sb("ut_b", [P, N], F32R, early)
            stack_a = sb("stack_a", [P, NC, P], F32, early)
            stack_b = sb("stack_b", [P, NC, P], F32, early)
        place = [(2, 2), (3, 3), (3, 2), (2, 3)]
        place += [n for n in FIRST_LOADS if n not in place]
        K = {n: sb(f"k_{n[0]}{n[1]}", [P, G, UW]) for n in place}
        A = sb("gate", [P, A_AT[NL]])
        xt = sb("xt", [P, NC, C])
        x_keep = sb("x_keep", [P, NC, C])
        z = sb("z", [P, NC, C])
        h = sb("h", [P, NC, C])
        y_sb = sb("y_sb", [P, 2, UW])
        ident = sb("ident", [P, P])
        deg_parts = sb("deg_parts", [P, NC, 5])
        deg = sb("deg", [P, NC])
        d = sb("d", [P, NC])
        f = sb("f", [P, NC])
        minus_half = sb("minus_half", [P, NC])
        mean = sb("mean", [P, NC])
        var = sb("var", [P, NC])
        rstd = sb("rstd", [P, NC])
        ws = sb("ws", [P, 1])
        u_sb = h[:, :, :].rearrange("p n c -> p (n c)")[:, 0:NC * R].rearrange("p (n r) -> p n r", n=NC)

        tw = ctx.enter_context(nc.psum_tensor("tw", [P, RING, UW], F32))
        kt = ctx.enter_context(nc.psum_tensor("kt", [P, RING, UW], F32))
        yp = ctx.enter_context(nc.psum_tensor("yp", [P, 2, UW], F32))
        y_bank = [(Y_AT + k) % RING for k in range(2)]

        def tw_bank(g):
            return (g if g < Y_AT else g + 2) % RING

        def h_last(k):
            return K[(1, 0)][:, k, :].rearrange("p (n c) -> p n c", c=C)

        loaded = {n: sem(f"loaded_{n[0]}{n[1]}") for n in LOADS}
        h_moved, ws_loaded, x_loaded = sem("h_moved"), sem("ws_loaded"), sem("x_loaded")
        x_kept = sem("x_kept")
        const_ready, ident_ready = sem("const_ready"), sem("ident_ready")
        high_ready, stack_ready = sem("high_ready"), sem("stack_ready")
        ut_done, ut_copied = sem("ut_done"), sem("ut_copied")
        uu_done, gate_ready = sem("uu_done"), sem("gate_ready")
        tw_done, sum_done, lower_done = sem("tw_done"), sem("sum_done"), sem("lower_done")
        kt_done, upper_done = sem("kt_done"), sem("upper_done")
        deg_summed, deg_ready, d_ready, z_ready = sem("deg_summed"), sem("deg_ready"), sem("d_ready"), sem("z_ready")
        prod_done, y_copied, yt_done = sem("prod_done"), sem("y_copied"), sem("yt_done")
        f_ready, y_scaled, h_ready = sem("f_ready"), sem("y_scaled"), sem("h_ready")
        h_summed, mean_ready, centered, squared = sem("h_summed"), sem("mean_ready"), sem("centered"), sem("squared")
        sq_summed, var_ready, rstd_ready, normed = sem("sq_summed"), sem("var_ready"), sem("rstd_ready"), sem("normed")

        UT_BANKS = [(yp, 0), (yp, 1), (tw, 0), (tw, 1), (tw, 2), (kt, 0), (kt, 1), (kt, 2)]
        first_unit = {m: min(q for q, pair in enumerate(PAIRS) for n in pair if n[1] == m) for m in range(NU_SIDE)}
        last_unit = {m: max(q for q, pair in enumerate(PAIRS) for n in pair if n[1] == m) for m in range(NU_SIDE)}

        def rows_of(t, b):
            return t[b, :, :].rearrange("(n p) c -> p n c", p=P)

        def per_row(v, n0, n1):
            return v[:, n0:n1].unsqueeze(2).broadcast_to([P, n1 - n0, C])

        block = ctx.enter_context(nc.Block())

        @block.sync
        def _(sp):
            def load_unit(b, n):
                i, j = n
                src = adj[b, i * UW:(i + 1) * UW, j * UW:(j + 1) * UW].rearrange("(g p) m -> p g m", p=P)
                sp.dma_start(K[n][:, :, :], src).then_inc(loaded[n], 16)

            sp.dma_start(u_sb, u.rearrange("(n p) r -> p n r", p=P)).then_inc(h_moved, 16)
            for k, n in enumerate(FIRST_LOADS):
                if k == X_AFTER:
                    sp.dma_start(xt[:, :, :], rows_of(x, 0)).then_inc(x_loaded, 16)
                if n in ((3, 2), (2, 3)):
                    sp.wait_ge(ut_done, 8)
                if n in ((2, 2), (3, 3)):
                    sp.wait_ge(uu_done, NL)
                load_unit(0, n)
            def load_units(b, units):
                passed = -1
                for n in units:
                    if PAIR_OF[n] > passed:
                        passed = PAIR_OF[n]
                        sp.wait_ge(prod_done, b * NQ + (passed + 1 - NQ))
                    load_unit(b, n)

            def store(b):
                sp.wait_ge(normed, b + 1)
                sp.dma_start(rows_of(out, b), h[:, :, :]).then_inc(h_moved, 16)

            load_units(1, LOADS)
            with sp.Fori(2, B) as b:
                load_units(b, LOADS)
                store(b - 2)
            store(B - 2)
            for k in range(2):
                sp.wait_ge(normed, B - 1 + (k + 1))
                sp.dma_start(rows_of(out, B - 1)[:, 8 * k:8 * k + 8, :], h_last(k)).then_inc(h_moved, 16)
            sp.wait_ge(h_moved, 16 * (B + 2))

        @block.gpsimd
        def _(pool):
            nc.gpsimd.memset(ident[:, :], 0.0).then_inc(const_ready, 1)
            pool.wait_ge(const_ready, 1)
            nc.gpsimd.affine_select(out=ident[:, :], in_=ident[:, :], compare_op=ALU.not_equal, fill=1.0,
                                    base=0, pattern=[[-1, P]], channel_multiplier=1).then_inc(ident_ready, 1)
            nc.gpsimd.memset(minus_half[:, :], -0.5).then_inc(const_ready, 1)
            pool.wait_ge(const_ready, 2)

            def add_x(b):
                pool.wait_ge(y_scaled, 2 * b + 2)
                pool.wait_ge(x_kept, b + 1)
                nc.gpsimd.tensor_tensor(h[:, :, :], h[:, :, :], x_keep[:, :, :], ALU.add).then_inc(h_ready, 1)

            def center(b):
                pool.wait_ge(mean_ready, b + 1)
                nc.gpsimd.tensor_tensor(h[:, :, :], h[:, :, :], per_row(mean, 0, NC),
                                        ALU.add).then_inc(centered, 1)

            def divide(b):
                pool.wait_ge(var_ready, b + 1)
                nc.gpsimd.tensor_tensor(rstd[:, :], var[:, :], minus_half[:, :], ALU.pow).then_inc(rstd_ready, 1)
                pool.wait_ge(rstd_ready, b + 1)
                nc.gpsimd.tensor_tensor(h[:, :, :], h[:, :, :], per_row(rstd, 0, NC),
                                        ALU.mult).then_inc(normed, 1)

            def degrees(b, k):
                pool.wait_ge(deg_ready, NZ * b + (k + 1))
                s = slice(*Z_GROUPS[k][:2])
                nc.gpsimd.tensor_tensor(d[:, s], deg[:, s], minus_half[:, s], ALU.pow).then_inc(d_ready, 1)

            def finish(b):
                add_x(b)
                center(b)
                divide(b)

            for b in range(2):
                for k in range(NZ):
                    degrees(b, k)
            with pool.Fori(2, B) as b:
                finish(b - 2)
                for k in range(NZ):
                    degrees(b, k)
            finish(B - 2)
            pool.wait_ge(normed, B - 1)
            for k in range(2):
                pool.wait_ge(var_ready, B - 1 + (k + 1))
                s = slice(8 * k, 8 * k + 8)
                nc.gpsimd.tensor_tensor(rstd[:, s], var[:, s], minus_half[:, s], ALU.pow).then_inc(rstd_ready, 1)

        @block.tensor
        def _(pe):
            def bank_free(b, place, stage):
                before = place - RING
                if before in (Y_AT, Y_AT + 1):
                    if stage == 2:
                        pe.wait_ge(y_scaled, 2 * b + (before - Y_AT - 3))
                elif before >= 0 or stage:
                    pe.wait_ge(sum_done, b * NL + (before + 1 if before < Y_AT else before - 1))

            def transpose_adjacency(b, s, r, stage):
                i, j = STEPS[s]
                g = s * G + r
                if r == 0:
                    pe.wait_ge(loaded[(j, i)], b * 16 + 16)
                bank_free(b, g if g < Y_AT else g + 2, stage)
                for c in range(lower_width(s, r) // P):
                    t = pe.transpose(tw[:, tw_bank(g), c * P:(c + 1) * P], K[(j, i)][:, c, r * P:(r + 1) * P],
                                     ident[:, :])
                t.then_inc(tw_done, 1)

            def transpose_rows(b, s, r, stage):
                i, j = STEPS[s]
                g = UPPER.index((s, r))
                if r == 0:
                    pe.wait_ge(lower_done, b * NL + G * (s + 1))
                if stage or g >= RING:
                    pe.wait_ge(upper_done, b * NU + (g + 1 - RING))
                chunks = range(G) if i != j else range(r + 1, G)
                for k, c in enumerate(chunks):
                    t = pe.transpose(kt[:, g % RING, k * P:(k + 1) * P], K[(i, j)][:, c, r * P:(r + 1) * P],
                                     ident[:, :])
                t.then_inc(kt_done, 1)

            def product(b, q, c, stage=2):
                if c == 0:
                    if q in Z_OF_PAIR:
                        pe.wait_ge(z_ready, NZ * b + (Z_OF_PAIR[q] + 1))
                    if q == 0 and stage == 0:
                        pe.wait_ge(gate_ready, NL)
                    elif q == 0:
                        pe.wait_ge(y_copied, 2 * b)
                for n, m in PAIRS[q]:
                    at = (m % 2) * C
                    t = pe.matmul(yp[at:at + C, m // 2, :], z[:, n * G + c, :], K[(n, m)][:, c, :],
                                  start=(q == first_unit[m] and c == 0), stop=(q == last_unit[m] and c == G - 1))
                if c == G - 1:
                    t.then_inc(prod_done, 1)

            def transpose_last_y(k):
                pe.wait_ge(y_copied, 2 * B - 2 + (k + 1))
                if k == 0:
                    pe.wait_ge(y_scaled, 2 * B - 2)
                for c in range(G):
                    t = pe.transpose(tw[:, y_bank[k], c * P:(c + 1) * P], K[(0, 0)][:, k, c * P:(c + 1) * P],
                                     ident[:, :])
                t.then_inc(yt_done, 1)

            def transpose_y(b, ending=False):
                for k in range(2):
                    pe.wait_ge(y_copied, 2 * b + (k + 1))
                    if not ending:
                        bank_free(b + 2, Y_AT + k, 2)
                    elif k == 0:
                        pe.wait_ge(sum_done, B * NL)
                    for c in range(G):
                        t = pe.transpose(tw[:, y_bank[k], c * P:(c + 1) * P], y_sb[:, k, c * P:(c + 1) * P], ident[:, :])
                    t.then_inc(yt_done, 1)

            def outer_product(g):
                s, r = LOWER[g]
                i, j = STEPS[s]
                if g >= 2:
                    pe.wait_ge(gate_ready, g - 1)
                w = lower_width(s, r)
                pe.matmul(yp[:, g % 2, 0:w], ut_a[:, (i * G + r) * P:(i * G + r + 1) * P],
                          ut_b[:, j * UW:j * UW + w], start=True, stop=True).then_inc(uu_done, 1)

            def steps(b, stage):
                carried = [(b - 1, q, c) for q in range(OWN, NQ) for c in range(G)]
                own = [(b, q, c) for q in range(OWN) for c in range(G)]
                for at in range(NL + G + 2):
                    if at == Y_AT and stage == 2:
                        transpose_y(b - 2)
                    if at < NL:
                        transpose_adjacency(b, *LOWER[at], stage)
                    if at < NL and stage == 0:
                        for g in range(gates_before(at), gates_before(at + 1)):
                            outer_product(g)
                    for part, row in zip(carried, CARRIED_ROWS):
                        if row == at and stage:
                            product(*part, stage=stage)
                    for part, row in zip(own, OWN_ROWS if stage else FIRST_OWN_ROWS):
                        if row == at:
                            product(*part, stage=stage)
                    for up in UPPER:
                        if at == (up[0] + 1) * G + up[1] + UPPER_LAG:
                            transpose_rows(b, *up, stage)

            pe.wait_ge(ident_ready, 1)
            for k, (dst, bank) in enumerate(UT_BANKS):
                if k < 2:
                    pe.wait_ge(stack_ready, k + 1)
                src = (stack_a, stack_b)[k % 2]
                for n in range(G):
                    t = pe.transpose(dst[:, bank, n * P:(n + 1) * P], src[:, G * (k // 2) + n, :], ident[:, :])
                t.then_inc(ut_done, 1)
            pe.wait_ge(ut_copied, 8)
            steps(0, 0)
            steps(1, 1)
            with pe.Fori(2, B) as b:
                steps(b, 2)
            transpose_y(B - 2, ending=True)
            for q, pair in enumerate(LAST_PAIRS):
                if q == 0:
                    pe.wait_ge(z_ready, NZ * B)
                for c in range(G):
                    if q == LAST_BANK0 and c == LAST_Y_CHUNK:
                        transpose_last_y(0)
                    for n, m in pair:
                        at = (m % 2) * C
                        t = pe.matmul(yp[at:at + C, m // 2, :], z[:, n * G + c, :], K[(n, m)][:, c, :],
                                      start=False, stop=(q in (LAST_BANK0 - 1, NQ - OWN - 1) and c == G - 1))
                t.then_inc(prod_done, 1)
            transpose_last_y(1)

        @block.scalar
        def _(act):
            def gate_row(g):
                w = lower_width(*LOWER[g])
                act.wait_ge(uu_done, g + 1)
                nc.scalar.activation(A[:, A_AT[g]:A_AT[g] + w], yp[:, g % 2, 0:w],
                                     ACT.Sigmoid).then_inc(gate_ready, 1)

            def upper_row(b, s, r):
                i, j = STEPS[s]
                g = UPPER.index((s, r))
                c0, part = (0, i) if i != j else (P * (r + 1), 4)
                n = j * G + r
                act.wait_ge(kt_done, b * NU + (g + 1))
                nc.scalar.activation(K[(j, i)][:, r, c0:UW], kt[:, g % RING, 0:UW - c0], ACT.Copy,
                                     accum_out=deg_parts[:, n, part:part + 1]).then_inc(upper_done, 1)

            def copy_y(b, early=False):
                act.wait_ge(prod_done, b * NQ + NQ)
                if not early:
                    act.wait_ge(sq_summed, b)
                for k in range(2):
                    nc.scalar.activation(y_sb[:, k, :], yp[:, k, :], ACT.Copy).then_inc(y_copied, 1)

            def square(b):
                act.wait_ge(centered, b + 1)
                nc.scalar.activation(y_sb[:, :, :].rearrange("p k w -> p (k w)"),
                                     h[:, :, :].rearrange("p n c -> p (n c)"), ACT.Square).then_inc(squared, 1)

            def keep_x(b, early=False):
                act.wait_ge(x_loaded, b * 16 + 16)
                if not early:
                    act.wait_ge(h_ready, b)
                nc.scalar.activation(x_keep[:, :, :].rearrange("p n c -> p (n c)"),
                                     xt[:, :, :].rearrange("p n c -> p (n c)"), ACT.Copy).then_inc(x_kept, 1)

            def load_x(b):
                act.dma_start(xt[:, :, :], rows_of(x, b)).then_inc(x_loaded, 16)

            def steps(b, stage):
                for at in range(NL + G + 1):
                    if stage == 0 and at < NL:
                        for g in range(gates_before(at), gates_before(at + 1)):
                            gate_row(g)
                    for up in UPPER:
                        if at == (up[0] + 1) * G + up[1] + UPPER_LAG:
                            upper_row(b, *up)
                    if at == KEEP_AT and stage:
                        keep_x(b - 1, early=(stage == 1))
                        act.wait_ge(z_ready, NZ * b)
                        act.wait_ge(x_kept, b)
                        load_x(b)
                    if at == SQUARE_AT and stage == 2:
                        square(b - 2)
                    if at == COPY_AT and stage:
                        copy_y(b - 1, early=(stage == 1))

            act.dma_start(ws[:, :], w_scale.partition_broadcast(P)).then_inc(ws_loaded, 16)
            for k in range(4):
                act.wait_ge(ut_done, 2 * k + 2)
                src, bank = UT_BANKS[2 * k + 1]
                nc.scalar.activation(ut_b[:, k * UW:(k + 1) * UW], src[:, bank, :], ACT.Copy).then_inc(ut_copied, 1)
            steps(0, 0)
            steps(1, 1)
            with act.Fori(2, B) as b:
                steps(b, 2)
            square(B - 2)
            for k in range(2):
                act.wait_ge(prod_done, B * NQ - (NQ - OWN - LAST_BANK0 if k == 0 else 0))
                nc.scalar.activation(K[(0, 0)][:, k, :], yp[:, k, :], ACT.Copy).then_inc(y_copied, 1)
                act.wait_ge(centered, B - 1 + (k + 1))
                nc.scalar.activation(K[(0, 1)][:, k, :], K[(1, 0)][:, k, :], ACT.Square).then_inc(squared, 1)

        @block.vector
        def _(dve):
            def add_row(b, g):
                s, r = LOWER[g]
                w = lower_width(s, r)
                row = K[STEPS[s]][:, r, 0:w]
                if r == 0:
                    dve.wait_ge(loaded[STEPS[s]], b * 16 + 16)
                dve.wait_ge(tw_done, b * NL + (g + 1))
                nc.vector.tensor_tensor(row, tw[:, tw_bank(g), 0:w], row, ALU.add).then_inc(sum_done, 1)

            def gate_product(b, g, first):
                s, r = LOWER[g]
                i, j = STEPS[s]
                w = lower_width(s, r)
                row = K[(i, j)][:, r, 0:w]
                if first:
                    dve.wait_ge(gate_ready, g + 1)
                dve.wait_ge(sum_done, b * NL + (g + 1))
                nc.vector.tensor_tensor_reduce(row, row, A[:, A_AT[g]:A_AT[g] + w], 1.0, 0.0, ALU.mult, ALU.add,
                                               deg_parts[:, i * G + r, j:j + 1]).then_inc(lower_done, 1)

            def sum_degrees(b, k):
                n0, n1, top = Z_GROUPS[k]
                dve.wait_ge(lower_done, b * NL + G * (top + 1))
                dve.wait_ge(upper_done, b * NU + UPPERS_TO[top])
                nc.vector.tensor_reduce(deg[:, n0:n1], deg_parts[:, n0:n1, :], AX_X, ALU.add).then_inc(deg_summed, 1)
                dve.wait_ge(deg_summed, NZ * b + (k + 1))
                nc.vector.tensor_scalar(deg[:, n0:n1], deg[:, n0:n1], 0.5, DEG_EPS, ALU.mult,
                                        ALU.max).then_inc(deg_ready, 1)

            def make_z(b, k, first):
                n0, n1, _ = Z_GROUPS[k]
                dve.wait_ge(d_ready, NZ * b + (k + 1))
                dve.wait_ge(x_loaded, b * 16 + 16)
                if not first:
                    dve.wait_ge(prod_done, b * NQ + (0 if k == NZ - 1 else OWN - NQ))
                nc.vector.tensor_tensor(z[:, n0:n1, :], xt[:, n0:n1, :], per_row(d, n0, n1),
                                        ALU.mult).then_inc(z_ready, 1)

            def scale(b):
                dve.wait_ge(d_ready, NZ * b + NZ)
                nc.vector.tensor_scalar(f[:, :], d[:, :], ws[:, 0:1], 0.5, ALU.mult, ALU.mult).then_inc(f_ready, 1)

            def scale_y(b):
                dve.wait_ge(f_ready, b + 1)
                dve.wait_ge(h_moved, b * 16 + 16)
                for k in range(2):
                    dve.wait_ge(yt_done, 2 * b + (k + 1))
                    src = tw[:, y_bank[k], :].rearrange("p (c half e) -> p half c e", c=G, half=2)
                    fk = f[:, 8 * k:8 * k + 8].rearrange("p (half c) -> p half c", half=2).unsqueeze(3)
                    dst = h[:, 8 * k:8 * k + 8, :].rearrange("p (half c) e -> p half c e", half=2)
                    nc.vector.tensor_tensor(dst, src, fk.broadcast_to([P, 2, G, C]),
                                            ALU.mult).then_inc(y_scaled, 1)

            def row_mean(b):
                dve.wait_ge(h_ready, b + 1)
                nc.vector.tensor_reduce(mean[:, :], h[:, :, :], AX_X, ALU.add).then_inc(h_summed, 1)
                dve.wait_ge(h_summed, b + 1)
                nc.vector.tensor_scalar(mean[:, :], mean[:, :], -1.0 / C, None, ALU.mult).then_inc(mean_ready, 1)

            def row_var(b):
                dve.wait_ge(squared, b + 1)
                nc.vector.tensor_reduce(var[:, :], y_sb[:, :, :].rearrange("p k (n c) -> p (k n) c", c=C), AX_X,
                                        ALU.add).then_inc(sq_summed, 1)
                dve.wait_ge(sq_summed, b + 1)
                nc.vector.tensor_scalar(var[:, :], var[:, :], 1.0 / C, LN_EPS, ALU.mult,
                                        ALU.add).then_inc(var_ready, 1)

            def steps(b, stage):
                z_rows = (DEG0_AT, Z0_AT, DEG1_AT, Z1_AT) if stage else (FIRST_DEG0_AT, FIRST_Z0_AT, FIRST_DEG1_AT,
                                                                         FIRST_Z1_AT)
                for g in range(NL + 1):
                    if g == Y_AT and stage == 2:
                        scale_y(b - 2)
                    if g < NL:
                        add_row(b, g)
                    if g:
                        gate_product(b, g - 1, stage == 0)
                    if g == MEAN_AT and stage == 2:
                        row_mean(b - 2)
                    if g == VAR_AT and stage == 2:
                        row_var(b - 2)
                    if g == z_rows[0]:
                        if stage:
                            scale(b - 1)
                        sum_degrees(b, 0)
                    if g == z_rows[1]:
                        make_z(b, 0, stage == 0)
                    if g == z_rows[2]:
                        sum_degrees(b, 1)
                    if g == z_rows[3]:
                        make_z(b, 1, stage == 0)
                sum_degrees(b, 2)
                make_z(b, 2, stage == 0)

            def finish_last(k):
                s, hk, done = slice(8 * k, 8 * k + 8), h_last(k), B - 1 + (k + 1)
                dve.wait_ge(yt_done, 2 * B - 2 + (k + 1))
                src = tw[:, y_bank[k], :].rearrange("p (c half e) -> p half c e", c=G, half=2)
                fk = f[:, s].rearrange("p (half c) -> p half c", half=2).unsqueeze(3)
                nc.vector.tensor_tensor(hk.rearrange("p (half c) e -> p half c e", half=2), src,
                                        fk.broadcast_to([P, 2, G, C]), ALU.mult).then_inc(y_scaled, 1)
                dve.wait_ge(y_scaled, 2 * B - 2 + (k + 1))
                nc.vector.tensor_tensor(hk, hk, xt[:, s, :], ALU.add).then_inc(h_ready, 1)
                dve.wait_ge(h_ready, done)
                if k == 0:
                    dve.wait_ge(centered, B - 1)
                nc.vector.tensor_reduce(mean[:, s], hk, AX_X, ALU.add).then_inc(h_summed, 1)
                dve.wait_ge(h_summed, done)
                nc.vector.tensor_scalar(mean[:, s], mean[:, s], -1.0 / C, None, ALU.mult).then_inc(mean_ready, 1)
                dve.wait_ge(mean_ready, done)
                nc.vector.tensor_tensor(hk, hk, per_row(mean, 8 * k, 8 * k + 8), ALU.add).then_inc(centered, 1)
                dve.wait_ge(squared, done)
                if k == 0:
                    dve.wait_ge(rstd_ready, B - 1)
                nc.vector.tensor_reduce(var[:, s], K[(0, 1)][:, k, :].rearrange("p (n c) -> p n c", c=C), AX_X,
                                        ALU.add).then_inc(sq_summed, 1)
                dve.wait_ge(sq_summed, done)
                nc.vector.tensor_scalar(var[:, s], var[:, s], 1.0 / C, LN_EPS, ALU.mult,
                                        ALU.add).then_inc(var_ready, 1)
                dve.wait_ge(rstd_ready, done)
                nc.vector.tensor_tensor(hk, hk, per_row(rstd, 8 * k, 8 * k + 8), ALU.mult).then_inc(normed, 1)

            nc.vector.memset(deg_parts[:, :, :], 0.0)
            nc.vector.memset(stack_a[:, :, 4 * R:P], 0.0)
            nc.vector.memset(stack_b[:, :, 4 * R:P], 0.0)
            dve.wait_ge(h_moved, 16)
            for part, t in ((0, stack_a), (2, stack_a), (0, stack_b), (1, stack_b)):
                last = nc.vector.tensor_copy(t[:, :, part * R:(part + 1) * R].bitcast(F32R), u_sb)
            last.then_inc(high_ready, 1)
            dve.wait_ge(high_ready, 1)
            high = stack_a[:, :, 0:R]
            for t, parts in ((stack_a, (1, 3)), (stack_b, (2, 3))):
                for part in parts:
                    last = nc.vector.tensor_tensor(t[:, :, part * R:(part + 1) * R], u_sb, high, ALU.subtract)
                last.then_inc(stack_ready, 1)
            for k in range(4):
                dve.wait_ge(ut_done, 2 * k + 1)
                src, bank = UT_BANKS[2 * k]
                nc.vector.tensor_copy(ut_a[:, k * UW:(k + 1) * UW], src[:, bank, :]).then_inc(ut_copied, 1)
            dve.wait_ge(ws_loaded, 16)
            steps(0, 0)
            steps(1, 1)
            with dve.Fori(2, B) as b:
                steps(b, 2)
            scale_y(B - 2)
            row_mean(B - 2)
            row_var(B - 2)
            scale(B - 1)
            dve.wait_ge(f_ready, B)
            for k in range(2):
                finish_last(k)


_INS = ["x", "adj", "L0_gnn_U", "L0_gnn_w_scale"]


def kernel(**inputs):
    import concourse.bacc as bacc
    from concourse.bass_utils import run_bass_kernel_spmd

    nc = bacc.Bacc("TRN2", target_bir_lowering=False, num_devices=1, dynamic_dma_scratch_size=4096)
    arrays, args = {}, []
    for name in _INS:
        a = np.ascontiguousarray(inputs[name])
        if a.ndim == 0:
            a = a.reshape(1)
        arrays[f"in_{name}_dram"] = a
        args.append(nc.dram_tensor(f"in_{name}_dram", a.shape, mybir.dt.from_np(a.dtype), kind="ExternalInput").ap())
    shape = inputs["x"].shape
    args.append(nc.dram_tensor("out_dram", shape, mybir.dt.from_np(np.dtype("float32")), kind="ExternalOutput").ap())
    bass_graph_resnorm_kernel(nc, *args)
    result = run_bass_kernel_spmd(nc, [arrays], core_ids=[0])
    return result.results[0]["out_dram"]
```
